# Optimizing a Trainium2 kernel written in Bass

```python
import numpy as np
import jax
import jax.numpy as jnp

def _softmax(x, axis=-1):
    return jax.nn.softmax(x, axis=axis)

def _gelu(x):
    return jax.nn.gelu(x, approximate=True)

def _silu(x):
    return jax.nn.silu(x)

def _sigmoid(x):
    return jax.nn.sigmoid(x)

def _layernorm(x, axis=-1, eps=1e-05):
    m = jnp.mean(x, axis=axis, keepdims=True)
    v = jnp.var(x, axis=axis, keepdims=True)
    return (x - m) / jnp.sqrt(v + eps)

def _scatter_add(tgt, idx, src, axis=0):
    return tgt.at[idx].add(src)

def _segment_sum(src, seg, n):
    return jax.ops.segment_sum(src, seg, n)
kernel_name = 'mk_rec_standalone_d1_rec_r8_f955ca'

def setup_inputs(seed: int=0):
    np.random.seed(seed)
    _w = jnp.asarray

    def _rec_inputs():
        import jax
        import jax.numpy as jnp
        _rk = jax.random.key(seed)
        r_user_rep = -0.000928989 + 1.00043 * jax.random.normal(jax.random.fold_in(_rk, 1), (512, 512), jnp.float32)
        r_indices = jnp.stack([jax.random.randint(jax.random.fold_in(jax.random.fold_in(_rk, 2), 0), (512,), 55, 99965, jnp.int32), jax.random.randint(jax.random.fold_in(jax.random.fold_in(_rk, 2), 1), (512,), 48, 12496, jnp.int32), jax.random.randint(jax.random.fold_in(jax.random.fold_in(_rk, 2), 2), (512,), 45, 99915, jnp.int32), jax.random.randint(jax.random.fold_in(jax.random.fold_in(_rk, 2), 3), (512,), 60, 99946, jnp.int32), jax.random.randint(jax.random.fold_in(jax.random.fold_in(_rk, 2), 4), (512,), 7, 99948, jnp.int32), jax.random.randint(jax.random.fold_in(jax.random.fold_in(_rk, 2), 5), (512,), 33, 99999, jnp.int32), jax.random.randint(jax.random.fold_in(jax.random.fold_in(_rk, 2), 6), (512,), 75, 99987, jnp.int32), jax.random.randint(jax.random.fold_in(jax.random.fold_in(_rk, 2), 7), (512,), 20, 99950, jnp.int32), jax.random.randint(jax.random.fold_in(jax.random.fold_in(_rk, 2), 8), (512,), 14, 99970, jnp.int32), jax.random.randint(jax.random.fold_in(jax.random.fold_in(_rk, 2), 9), (512,), 36, 99989, jnp.int32), jax.random.randint(jax.random.fold_in(jax.random.fold_in(_rk, 2), 10), (512,), 4, 99993, jnp.int32), jax.random.randint(jax.random.fold_in(jax.random.fold_in(_rk, 2), 11), (512,), 56, 99973, jnp.int32), jax.random.randint(jax.random.fold_in(jax.random.fold_in(_rk, 2), 12), (512,), 15, 99974, jnp.int32), jax.random.randint(jax.random.fold_in(jax.random.fold_in(_rk, 2), 13), (512,), 97, 99986, jnp.int32), jax.random.randint(jax.random.fold_in(jax.random.fold_in(_rk, 2), 14), (512,), 23, 99998, jnp.int32), jax.random.randint(jax.random.fold_in(jax.random.fold_in(_rk, 2), 15), (512,), 57, 99994, jnp.int32), jax.random.randint(jax.random.fold_in(jax.random.fold_in(_rk, 2), 16), (512,), 6, 12495, jnp.int32), jax.random.randint(jax.random.fold_in(jax.random.fold_in(_rk, 2), 17), (512,), 1, 12469, jnp.int32), jax.random.randint(jax.random.fold_in(jax.random.fold_in(_rk, 2), 18), (512,), 24, 99879, jnp.int32), jax.random.randint(jax.random.fold_in(jax.random.fold_in(_rk, 2), 19), (512,), 200, 99973, jnp.int32), jax.random.randint(jax.random.fold_in(jax.random.fold_in(_rk, 2), 20), (512,), 89, 12495, jnp.int32), jax.random.randint(jax.random.fold_in(jax.random.fold_in(_rk, 2), 21), (512,), 68, 99881, jnp.int32), jax.random.randint(jax.random.fold_in(jax.random.fold_in(_rk, 2), 22), (512,), 2, 99901, jnp.int32), jax.random.randint(jax.random.fold_in(jax.random.fold_in(_rk, 2), 23), (512,), 74, 12479, jnp.int32), jax.random.randint(jax.random.fold_in(jax.random.fold_in(_rk, 2), 24), (512,), 53, 99950, jnp.int32), jax.random.randint(jax.random.fold_in(jax.random.fold_in(_rk, 2), 25), (512,), 69, 99982, jnp.int32), jax.random.randint(jax.random.fold_in(jax.random.fold_in(_rk, 2), 26), (512,), 175, 99910, jnp.int32), jax.random.randint(jax.random.fold_in(jax.random.fold_in(_rk, 2), 27), (512,), 135, 99953, jnp.int32), jax.random.randint(jax.random.fold_in(jax.random.fold_in(_rk, 2), 28), (512,), 19, 99994, jnp.int32), jax.random.randint(jax.random.fold_in(jax.random.fold_in(_rk, 2), 29), (512,), 122, 99955, jnp.int32), jax.random.randint(jax.random.fold_in(jax.random.fold_in(_rk, 2), 30), (512,), 8, 99927, jnp.int32), jax.random.randint(jax.random.fold_in(jax.random.fold_in(_rk, 2), 31), (512,), 13, 99979, jnp.int32), jax.random.randint(jax.random.fold_in(jax.random.fold_in(_rk, 2), 32), (512,), 120, 99930, jnp.int32), jax.random.randint(jax.random.fold_in(jax.random.fold_in(_rk, 2), 33), (512,), 5, 99972, jnp.int32), jax.random.randint(jax.random.fold_in(jax.random.fold_in(_rk, 2), 34), (512,), 81, 99879, jnp.int32), jax.random.randint(jax.random.fold_in(jax.random.fold_in(_rk, 2), 35), (512,), 2, 99958, jnp.int32), jax.random.randint(jax.random.fold_in(jax.random.fold_in(_rk, 2), 36), (512,), 2, 99998, jnp.int32), jax.random.randint(jax.random.fold_in(jax.random.fold_in(_rk, 2), 37), (512,), 57, 99983, jnp.int32), jax.random.randint(jax.random.fold_in(jax.random.fold_in(_rk, 2), 38), (512,), 63, 99987, jnp.int32), jax.random.randint(jax.random.fold_in(jax.random.fold_in(_rk, 2), 39), (512,), 35, 99956, jnp.int32), jax.random.randint(jax.random.fold_in(jax.random.fold_in(_rk, 2), 40), (512,), 1, 12490, jnp.int32), jax.random.randint(jax.random.fold_in(jax.random.fold_in(_rk, 2), 41), (512,), 27, 99969, jnp.int32), jax.random.randint(jax.random.fold_in(jax.random.fold_in(_rk, 2), 42), (512,), 0, 12495, jnp.int32), jax.random.randint(jax.random.fold_in(jax.random.fold_in(_rk, 2), 43), (512,), 25, 99926, jnp.int32), jax.random.randint(jax.random.fold_in(jax.random.fold_in(_rk, 2), 44), (512,), 28, 99839, jnp.int32), jax.random.randint(jax.random.fold_in(jax.random.fold_in(_rk, 2), 45), (512,), 5, 99986, jnp.int32), jax.random.randint(jax.random.fold_in(jax.random.fold_in(_rk, 2), 46), (512,), 20, 99986, jnp.int32), jax.random.randint(jax.random.fold_in(jax.random.fold_in(_rk, 2), 47), (512,), 4, 99981, jnp.int32), jax.random.randint(jax.random.fold_in(jax.random.fold_in(_rk, 2), 48), (512,), 55, 99954, jnp.int32), jax.random.randint(jax.random.fold_in(jax.random.fold_in(_rk, 2), 49), (512,), 21, 99978, jnp.int32)], axis=1)
        return (r_user_rep, r_indices)
    r_user_rep, r_indices = _rec_inputs()

    def _L0_rec_setup():
        import jax, jax.numpy as jnp
        import numpy as np
        key = jax.random.key(seed)
        ks = jax.random.split(key, 6)
        B, K, V, H = (256, 50, 12500, 512)
        return {'user_rep': jax.random.normal(ks[0], (B, H), dtype=jnp.float32), 'indices': jax.random.randint(ks[1], (B, K), 0, V, dtype=jnp.int64), 'item_embeddings': jax.random.normal(ks[2], (V, H), dtype=jnp.float32), 'W_fuse': jax.random.normal(ks[3], (2 * H, H), dtype=jnp.float32) * (1.0 / np.sqrt(2 * H)), 'b_fuse': jnp.zeros((H,), dtype=jnp.float32), 'W_proj': jax.random.normal(ks[4], (H, V), dtype=jnp.float32) * (1.0 / np.sqrt(H)), 'b_proj': jnp.zeros((V,), dtype=jnp.float32)}
    _L0_rec_all = _L0_rec_setup()
    _L0_rec_in = {k: v for k, v in _L0_rec_all.items() if k in ('item_embeddings', 'W_fuse', 'b_fuse', 'W_proj', 'b_proj')}
    del _L0_rec_all
    return {'r_user_rep': r_user_rep, 'r_indices': r_indices, 'L0_rec_item_embeddings': _L0_rec_in['item_embeddings'], 'L0_rec_W_fuse': _L0_rec_in['W_fuse'], 'L0_rec_b_fuse': _L0_rec_in['b_fuse'], 'L0_rec_W_proj': _L0_rec_in['W_proj'], 'L0_rec_b_proj': _L0_rec_in['b_proj']}

def reference(r_user_rep, r_indices, L0_rec_item_embeddings, L0_rec_W_fuse, L0_rec_b_fuse, L0_rec_W_proj, L0_rec_b_proj):
    import jax
    import jax.numpy as jnp

    def _L0_rec_ref(user_rep, indices, item_embeddings, W_fuse, b_fuse, W_proj, b_proj):
        import jax, jax.numpy as jnp
        import numpy as np
        retrieved = jnp.mean(item_embeddings[indices], axis=1)
        fused_input = jnp.concatenate([user_rep, retrieved], axis=1)
        fused_rep = fused_input @ W_fuse + b_fuse
        logits = fused_rep @ W_proj + b_proj
        return logits
    y = _L0_rec_ref(r_user_rep, r_indices, L0_rec_item_embeddings, L0_rec_W_fuse, L0_rec_b_fuse, L0_rec_W_proj, L0_rec_b_proj)
    return y

_drawn_inputs = setup_inputs


def setup_inputs(seed=0):
    import zlib

    import numpy as np

    out = dict(_drawn_inputs(seed))
    spreads = {'L0_rec_b_fuse': (0.0, 0.1), 'L0_rec_b_proj': (0.0, 0.1)}
    factors = {}
    for name, (base, spread) in spreads.items():
        noise = np.random.default_rng([zlib.crc32(name.encode()), seed]).standard_normal(out[name].shape)
        drawn = base * np.exp(spread * noise) if base else spread * noise
        out[name] = jnp.asarray(drawn.astype(out[name].dtype))
    for name, factor in factors.items():
        out[name] = (out[name] * factor).astype(out[name].dtype)
    return out
```

```python
from contextlib import ExitStack

import concourse.bass as bass
from concourse import mybir

P = 128
F32 = mybir.dt.float32
F32R = mybir.dt.float32r
I32 = mybir.dt.int32
ALU = mybir.AluOpType
ACT = mybir.ActivationFunctionType
AX_X = mybir.AxisListType.X

ACC_SLOTS = 5
LAPS = 2
TURN = LAPS * ACC_SLOTS
MIN_TURNS = 2
CHUNK = 500
RESIDENT = 8
ROUND_F32 = float(2 ** 23)


def retrieval_scores(nc, user, indices, table, w_fuse, b_fuse, w_proj, b_proj, out):
    B, H = user.shape
    K = indices.shape[1]
    V = table.shape[0]
    TILES = B // P
    HK = H // P
    CHUNKS = V // CHUNK
    LAST = V - 1
    PAD = (K + 7) // 8 * 8
    PAIRS = RESIDENT // 2
    PHASE1 = TILES * RESIDENT
    assert B % P == 0 and H % P == 0 and V % CHUNK == 0 and K % TURN == 0 and TILES == 4 and HK == 4
    assert RESIDENT % 2 == 0 and (CHUNKS - 1) % RESIDENT == 0 and CHUNKS > 2 * RESIDENT

    idx_dram = indices.rearrange("(t p) k -> p t k", p=P)
    user_dram = user.rearrange("(t p) h -> p t h", p=P)
    wf_dram = w_fuse.rearrange("(s k p) n -> s p k n", s=2, p=P)
    bf_dram = b_fuse.rearrange("(k p) -> p k", p=P)
    wp_dram = w_proj.rearrange("(k p) v -> k p v", p=P)
    bp_dram = b_proj.rearrange("(a v) -> a v", a=1)
    out_dram = out.rearrange("(t p) v -> t p v", p=P)

    with ExitStack() as ctx:
        def sb(name, shape, dt=F32):
            return ctx.enter_context(nc.sbuf_tensor(name, shape, dt))

        def sem(name):
            return ctx.enter_context(nc.semaphore(name))

        w_hi = sb("w_hi", [P, RESIDENT, HK, CHUNK], F32R)
        w_lo = sb("w_lo", [P, RESIDENT, HK, CHUNK], F32R)
        w_raw = sb("w_raw", [P, HK, CHUNK])
        f_hi = sb("f_hi", [P, TILES, HK, P], F32R)
        f_lo = sb("f_lo", [P, TILES, HK, P], F32R)
        acc = sb("acc", [P, 2, ACC_SLOTS, H])
        early = sb("early", [P, 2, HK, 512])
        user_t = early[:, 0, :, 0:B]
        wf_user = early[:, 1, :, 0:H]
        bias = early[:, :, :, :].rearrange("p a k n -> p (a k) n")
        user_sb = acc[:, 1, 0:TILES, :]
        wf_ret = sb("wf_ret", [P, HK, H])
        ret_t = sb("ret_t", [P, HK, P])
        last_row = sb("last_row", [P, H])
        bf_col = sb("bf_col", [P, HK])
        out_sb = sb("out_sb", [P, TILES, CHUNK])
        key = out_sb[:, 0, 0:TILES * K].rearrange("p (t k) -> p t k", k=K)
        flags = out_sb[:, 1, 0:TILES * K].rearrange("p (t k) -> p t k", k=K)
        key_left = out_sb[:, 2, 0:2 * K].rearrange("p (a k) -> p a k", k=K)
        ones_row = out_sb[0:1, 3, 0:P]
        ident = sb("ident", [P, P])
        idx = sb("idx", [P, TILES, K], I32)
        key_sorted = sb("key_sorted", [P, PAD])
        rows = sb("rows", [P, TILES, PAD], I32)
        lap_rows = sb("lap_rows", [P, LAPS, ACC_SLOTS], I32)
        n_inner = sb("n_inner", [P, TILES])
        turns_f = sb("turns_f", [1, TILES])
        turns_i = sb("turns_i", [1, TILES], I32)
        n_left = sb("n_left", [P, TILES])

        banks = [ctx.enter_context(nc.psum_tensor(f"bank{i}", [P, 512], F32)) for i in range(8)]
        fused_ps = banks[0:HK]
        tr_ps = banks[4]
        pair_ps = banks[5:7]
        small_ps = banks[7]
        phase2_ps = fused_ps

        idx_landed = sem("idx_landed")
        user_landed = sem("user_landed")
        wf_user_landed = sem("wf_user_landed")
        wf_ret_landed = sem("wf_ret_landed")
        last_landed = sem("last_landed")
        bf_landed = sem("bf_landed")
        w_landed = [sem(f"w_landed{k}") for k in range(HK)]
        bias_first = sem("bias_first")
        bias_landed = sem("bias_landed")
        out_stored = [sem(f"out_stored{t}") for t in range(TILES)]
        gathered = [[sem(f"gathered{t}_{s}") for s in range(ACC_SLOTS)] for t in range(TILES)]
        lap_rows_set = [sem(f"lap_rows_set{t}") for t in range(TILES)]
        sum_landed = sem("sum_landed")
        pool_const = sem("pool_const")
        ident_ready = sem("ident_ready")
        ones_ready = sem("ones_ready")
        dve_step = sem("dve_step")
        rows_ready = sem("rows_ready")
        counted = sem("counted")
        counts_moved = sem("counts_moved")
        turns_ready = sem("turns_ready")
        turns_spread = sem("turns_spread")
        user_turned = sem("user_turned")
        user_t_ready = sem("user_t_ready")
        user_fused = sem("user_fused")
        summed = sem("summed")
        ret_turned = sem("ret_turned")
        ret_ready = sem("ret_ready")
        fused = sem("fused")
        f_hi_ready = sem("f_hi_ready")
        f_ready = sem("f_ready")
        hi_ready = sem("hi_ready")
        lo_ready = sem("lo_ready")
        projected = sem("projected")
        evacuated = sem("evacuated")

        def out_slot(t, e):
            return 2 * (t % 2) + e

        block = ctx.enter_context(nc.Block())

        @block.sync
        def _(sp):
            def load_unit(c, k, wait=True):
                if wait:
                    sp.wait_ge(lo_ready, HK * c - HK + k + 1)
                sp.dma_start(w_raw[:, k, :], wp_dram[k, :, bass.ds(c * CHUNK, CHUNK)]).then_inc(w_landed[k], 16)

            def load_bias(c, slot):
                sp.dma_start(bias[:, bass.ds(slot, 1), 0:CHUNK],
                             bp_dram[:, bass.ds(c * CHUNK, CHUNK)].unsqueeze(1).to_broadcast([P, 1, CHUNK]))\
                  .then_inc(bias_landed, 16)

            def store(t, c, group, slot):
                sp.wait_ge(evacuated, group + 1)
                sp.dma_start(out_dram[t, :, bass.ds(c * CHUNK, CHUNK)], out_sb[:, slot, :])\
                  .then_inc(out_stored[slot], 16)

            sp.dma_start(idx[:], idx_dram).then_inc(idx_landed, 16)
            for k in range(HK):
                load_unit(0, k, wait=False)
            with sp.Fori(1, RESIDENT) as c:
                for k in range(HK):
                    load_unit(c, k)
            for k in range(HK):
                load_unit(RESIDENT, k)

            sp.wait_ge(user_fused, HK)
            sp.dma_start(bias[:, :, 0:CHUNK],
                         bp_dram[:, 0:RESIDENT * CHUNK].rearrange("a (c n) -> a c n", n=CHUNK)
                         .to_broadcast([P, RESIDENT, CHUNK])).then_inc(bias_first, 16)

            for t in range(TILES - 1):
                with sp.Fori(0, PAIRS) as j:
                    for e in range(2):
                        store(t, 2 * j + e, t * RESIDENT + 2 * j + e, out_slot(t, e))
            t = TILES - 1
            for j in range(PAIRS):
                for e in range(2):
                    store(t, 2 * j + e, t * RESIDENT + 2 * j + e, out_slot(t, e))
                load_unit(RESIDENT + 1, j)
                if j == 0:
                    load_bias(RESIDENT, 0)
                if j == 1:
                    sp.wait_ge(bias_landed, 16)
                    load_bias(RESIDENT + 1, 1)

            def phase2(c, slot_after_next, more):
                for t in range(TILES):
                    store(t, c, TILES * c + t, t)
                    if more:
                        load_unit(c + 2, t)
                        if t == 0:
                            sp.wait_ge(bias_landed, 16 * (c + 2 - RESIDENT))
                            load_bias(c + 2, slot_after_next)

            for base in range(RESIDENT, CHUNKS - 1, RESIDENT):
                rounds = [(0, RESIDENT - 2, 2), (RESIDENT - 2, RESIDENT, 2 - RESIDENT)]
                for a, b, d in rounds:
                    if base + b + 2 <= CHUNKS:
                        with sp.Fori(a, b) as j:
                            phase2(base + j, j + d, True)
                    else:
                        for j in range(a, b):
                            phase2(base + j, j + d, base + j + 2 < CHUNKS)
            phase2(CHUNKS - 1, 0, False)
            for t in range(TILES):
                sp.wait_ge(out_stored[t], 16 * CHUNKS)

        @block.gpsimd
        def _(pool):
            nc.gpsimd.memset(ident[:], 0.0).then_inc(pool_const, 1)
            nc.gpsimd.memset(ones_row, 1.0).then_inc(ones_ready, 1)
            pool.wait_ge(pool_const, 1)
            nc.gpsimd.affine_select(out=ident[:], in_=ident[:], compare_op=ALU.not_equal, fill=1.0, base=0,
                                    pattern=[[-1, P]], channel_multiplier=1).then_inc(ident_ready, 1)

            def gather(t, s, column, **how):
                return nc.gpsimd.indirect_dma_start(
                    out=acc[:, t % 2, s, :], out_offset=None, in_=table,
                    in_offset=bass.IndirectOffsetOnAxis(ap=column, axis=0), **how)

            for t in range(TILES):
                pool.wait_ge(rows_ready, t + 1)
                if t == 1:
                    pool.wait_ge(user_turned, HK)
                if t >= 2:
                    pool.wait_ge(ret_turned, t - 1)
                for s in range(ACC_SLOTS):
                    gather(t, s, rows[:, t, s:s + 1]).then_inc(gathered[t][s], 16)
                for s in range(ACC_SLOTS):
                    pool.wait_ge(gathered[t][s], 16)
                    gather(t, s, rows[:, t, ACC_SLOTS + s:ACC_SLOTS + s + 1], compute_op=ALU.add)\
                        .then_inc(gathered[t][s], 16)
                if t == 0:
                    pool.wait_ge(turns_ready, 1)
                turns = pool.value_load(turns_i[0:1, t:t + 1], min_val=MIN_TURNS, max_val=K // TURN)
                with pool.Fori(1, turns) as turn:
                    for lap in range(LAPS):
                        first = (turn * LAPS + lap) * ACC_SLOTS
                        nc.gpsimd.tensor_copy(lap_rows[:, lap, :], rows[:, t, bass.ds(first, ACC_SLOTS)])\
                          .then_inc(lap_rows_set[t], 1)
                        pool.wait_ge(lap_rows_set[t], turn * LAPS + (lap + 1 - LAPS))
                        for s in range(ACC_SLOTS):
                            pool.wait_ge(gathered[t][s], turn * (16 * LAPS) + 16 * lap)
                            pool.sem_inc(sum_landed, 1)
                            gather(t, s, lap_rows[:, lap, s:s + 1], compute_op=ALU.add).then_inc(gathered[t][s], 16)

        @block.scalar
        def _(act):
            def split_hi(c, slot, landed, free=None):
                for k in range(HK):
                    act.wait_ge(w_landed[k], landed)
                    if free is not None and k == 0:
                        act.wait_ge(projected, free)
                    nc.scalar.copy(w_hi[:, bass.ds(slot, 1), k, :], w_raw[:, k:k + 1, :]).then_inc(hi_ready, 1)

            act.dma_start(user_sb, user_dram).then_inc(user_landed, 16)
            act.dma_start(wf_user, wf_dram[0]).then_inc(wf_user_landed, 16)
            act.dma_start(wf_ret[:], wf_dram[1]).then_inc(wf_ret_landed, 16)
            act.dma_start(last_row[:], table[LAST:V, :].to_broadcast([P, H])).then_inc(last_landed, 16)
            with nc.allow_non_contiguous_dma(reason="512 words, once"):
                act.dma_start(bf_col[:], bf_dram).then_inc(bf_landed, 16)

            for k in range(HK):
                act.wait_ge(user_turned, k + 1)
                nc.scalar.copy(user_t[:, k, :], banks[k][:, :]).then_inc(user_t_ready, 1)
            with act.Fori(0, RESIDENT) as c:
                split_hi(c, c, 16 * c + 16)

            def fuse(t):
                act.wait_ge(ret_turned, t + 1)
                if t:
                    act.wait_ge(fused, HK * t)
                nc.scalar.mul(ret_t[:], tr_ps[:, :].rearrange("p (k n) -> p k n", k=HK), 1.0 / K)\
                  .then_inc(ret_ready, 1)
                if t == 0:
                    act.wait_ge(bf_landed, 16)
                for k in range(HK):
                    act.wait_ge(fused, HK * t + k + 1)
                    nc.scalar.activation(f_hi[:, t, k, :], fused_ps[k][:, t * P:(t + 1) * P], ACT.Identity,
                                         bias=bf_col[:, k:k + 1]).then_inc(f_hi_ready, 1)

            for t in range(TILES):
                fuse(t)
            last = TILES - 1
            split_hi(RESIDENT, 0, 16 * (RESIDENT + 1), last * RESIDENT + 1)
            with act.Fori(1, RESIDENT) as j:
                split_hi(j + RESIDENT, j, 16 * j + 16 * (RESIDENT + 1), last * RESIDENT + 1 + j)
            with act.Fori(0, RESIDENT) as j:
                split_hi(j + 2 * RESIDENT, j, 16 * j + 16 * (2 * RESIDENT + 1), TILES * j + PHASE1 + TILES)
            split_hi(CHUNKS - 1, 0, 16 * CHUNKS, PHASE1 + TILES * RESIDENT + TILES)

        @block.vector
        def _(dve):
            steps = [0]

            def then(instruction):
                steps[0] += 1
                instruction.then_inc(dve_step, 1)
                dve.wait_ge(dve_step, steps[0])

            def split_lo(slot, k, count):
                dve.wait_ge(hi_ready, count)
                nc.vector.tensor_tensor(w_lo[:, bass.ds(slot, 1), k, :], w_raw[:, k:k + 1, :],
                                        w_hi[:, bass.ds(slot, 1), k, :].bitcast(F32), ALU.subtract)\
                  .then_inc(lo_ready, 1)

            def sort(t):
                src = key[:, t, :]
                for n in range(PAD // 8):
                    top = key_sorted[:, 8 * n:8 * n + 8]
                    then(nc.vector.max(top, src))
                    if n < PAD // 8 - 1:
                        rest = key_left[:, n % 2, :]
                        then(nc.vector.match_replace(out=rest, in_to_replace=top, in_values=src, imm_value=0.0))
                        src = rest
                nc.vector.tensor_scalar(rows[:, t, :], key_sorted[:], -1.0, float(LAST), ALU.mult, ALU.add)\
                  .then_inc(rows_ready, 1)
                dve.wait_ge(rows_ready, t + 1)

            dve.wait_ge(idx_landed, 16)
            then(nc.vector.tensor_scalar(key, idx[:], 0.0, float(V), ALU.is_lt, ALU.mult))
            then(nc.vector.tensor_tensor(key, key, idx[:], ALU.add))
            then(nc.vector.tensor_scalar(key, key, 0.0, float(LAST), ALU.max, ALU.min))
            then(nc.vector.tensor_scalar(key, key, -1.0, float(LAST), ALU.mult, ALU.add))
            sort(0)
            then(nc.vector.tensor_scalar(flags, key, 0.0, None, ALU.is_gt))
            nc.vector.tensor_reduce(n_inner[:], flags, AX_X, ALU.add).then_inc(counted, 1)
            dve.wait_ge(counts_moved, 1)
            then(nc.vector.tensor_reduce(turns_f[:], small_ps[0:1, :].rearrange("a (t p) -> a t p", p=P), AX_X, ALU.max))
            then(nc.vector.tensor_scalar(turns_f[:], turns_f[:], float(TURN * MIN_TURNS), 1.0 / TURN,
                                         ALU.max, ALU.mult))
            then(nc.vector.tensor_scalar(turns_f[:], turns_f[:], 0.5 - 0.5 / TURN, ROUND_F32, ALU.add, ALU.add))
            then(nc.vector.tensor_scalar(turns_f[:], turns_f[:], ROUND_F32, None, ALU.subtract))
            nc.vector.tensor_copy(turns_i[:], turns_f[:]).then_inc(turns_ready, 1)
            dve.wait_ge(turns_spread, 1)
            then(nc.vector.tensor_scalar(n_left[:], small_ps[:, 0:TILES], -float(TURN), float(K),
                                         ALU.mult, ALU.add))
            for t in range(1, TILES):
                sort(t)

            with dve.Fori(0, RESIDENT) as c:
                for k in range(HK):
                    split_lo(c, k, HK * c + k + 1)

            def sum_half(t, half):
                if half == 0:
                    turns = dve.value_load(turns_i[0:1, t:t + 1], min_val=MIN_TURNS, max_val=K // TURN)
                    for s in range(ACC_SLOTS):
                        dve.wait_ge(gathered[t][s], turns * (16 * LAPS))
                cols = slice(half * H // 2, (half + 1) * H // 2)
                then(nc.vector.tensor_reduce(small_ps[:, cols],
                                             acc[:, t % 2, :, cols].rearrange("p s h -> p h s"), AX_X, ALU.add))

            def add_last(t):
                if t == 0:
                    dve.wait_ge(last_landed, 16)
                nc.vector.scalar_tensor_tensor(acc[:, t % 2, 0, :], last_row[:], n_left[:, t:t + 1],
                                               small_ps[:, 0:H], ALU.mult, ALU.add).then_inc(summed, 1)

            def fused_lo(t):
                if t == 0:
                    dve.wait_ge(bf_landed, 16)
                for k in range(HK):
                    dve.wait_ge(f_hi_ready, HK * t + k + 1)
                    nc.vector.scalar_tensor_tensor(f_lo[:, t, k, :], fused_ps[k][:, t * P:(t + 1) * P],
                                                   bf_col[:, k:k + 1], f_hi[:, t, k, :].bitcast(F32),
                                                   ALU.add, ALU.subtract).then_inc(f_ready, 1)

            def evacuate(ps, group, slot, bias_slot, stored=None):
                dve.wait_ge(projected, group + 1)
                if stored is not None:
                    dve.wait_ge(out_stored[slot], stored)
                nc.vector.tensor_tensor(out_sb[:, slot:slot + 1, :], ps[:, 0:CHUNK].unsqueeze(1),
                                        bias[:, bass.ds(bias_slot, 1), 0:CHUNK], ALU.add).then_inc(evacuated, 1)

            def evacuate_pair(t, j, parts=(0, 1)):
                for e in parts:
                    first = t < 2 and type(j) is int and j == 0
                    evacuate(pair_ps[e], t * RESIDENT + 2 * j + e, out_slot(t, e), 2 * j + e,
                             None if first else 16 * (t // 2 * PAIRS + j))

            sum_half(0, 0)
            sum_half(0, 1)
            add_last(0)
            fused_lo(0)
            dve.wait_ge(bias_first, 16)
            for t in range(TILES - 1):
                if t < 2:
                    evacuate_pair(t, 0)
                with dve.Fori(1 if t < 2 else 0, PAIRS - 2) as j:
                    evacuate_pair(t, j)
                evacuate_pair(t, PAIRS - 2, (0,))
                sum_half(t + 1, 0)
                evacuate_pair(t, PAIRS - 2, (1,))
                sum_half(t + 1, 1)
                add_last(t + 1)
                evacuate_pair(t, PAIRS - 1)
                fused_lo(t + 1)
            for j in range(PAIRS):
                evacuate_pair(TILES - 1, j)
                split_lo(0, j, HK * RESIDENT + j + 1)

            def phase2(c, slot, next_slot):
                dve.wait_ge(bias_landed, 16 * (c - RESIDENT + 1))
                for t in range(TILES):
                    evacuate(phase2_ps[t], TILES * c + t, t, slot, 16 * c)
                    if next_slot is not None:
                        split_lo(next_slot, t, HK * (c + 1) + t + 1)

            for base in range(RESIDENT, CHUNKS - 1, RESIDENT):
                with dve.Fori(0, RESIDENT - 1) as j:
                    phase2(base + j, j, j + 1)
                phase2(base + RESIDENT - 1, RESIDENT - 1, 0)
            phase2(CHUNKS - 1, 0, None)

        @block.tensor
        def _(pe):
            pe.wait_ge(ident_ready, 1)
            pe.wait_ge(user_landed, 16)
            for k in range(HK):
                for t in range(TILES):
                    m = nc.tensor.transpose(banks[k][:, t * P:(t + 1) * P], user_sb[:, t, k * P:(k + 1) * P], ident[:])
                m.then_inc(user_turned, 1)

            pe.wait_ge(counted, 1)
            for t in range(TILES):
                m = nc.tensor.matmul(small_ps[0:1, t * P:(t + 1) * P], n_inner[:, t:t + 1], ident[:],
                                     start=True, stop=True)
            m.then_inc(counts_moved, 1)
            pe.wait_ge(ones_ready, 1)
            pe.wait_ge(turns_ready, 1)
            nc.tensor.matmul(small_ps[:, 0:TILES], ones_row, turns_f[:], start=True, stop=True).then_inc(turns_spread, 1)

            pe.wait_ge(user_t_ready, HK)
            pe.wait_ge(wf_user_landed, 16)
            for n in range(HK):
                for k in range(HK):
                    m = nc.tensor.matmul(fused_ps[n][:, :], wf_user[:, k, n * P:(n + 1) * P], user_t[:, k, :],
                                         start=(k == 0), stop=(k == HK - 1))
                m.then_inc(user_fused, 1)

            def turn_sum(t):
                pe.wait_ge(summed, t + 1)
                if t:
                    pe.wait_ge(ret_ready, t)
                for k in range(HK):
                    m = nc.tensor.transpose(tr_ps[:, k * P:(k + 1) * P], acc[:, t % 2, 0, k * P:(k + 1) * P], ident[:])
                m.then_inc(ret_turned, 1)

            def fuse(t):
                pe.wait_ge(ret_ready, t + 1)
                if t == 0:
                    pe.wait_ge(wf_ret_landed, 16)
                for n in range(HK):
                    for k in range(HK):
                        m = nc.tensor.matmul(fused_ps[n][:, t * P:(t + 1) * P], wf_ret[:, k, n * P:(n + 1) * P],
                                             ret_t[:, k, :], start=False, stop=(k == HK - 1), skip_group_check=True)
                    m.then_inc(fused, 1)

            def project(t, slot, ps, free=None):
                if free is not None:
                    pe.wait_ge(evacuated, free)
                for k in range(HK):
                    hi, lo = w_hi[:, bass.ds(slot, 1), k, :], w_lo[:, bass.ds(slot, 1), k, :]
                    for f, w, first in ((f_hi, hi, k == 0), (f_hi, lo, False), (f_lo, hi, False)):
                        m = nc.tensor.matmul(ps[:, 0:CHUNK].unsqueeze(1), f[:, t, k, :], w, start=first,
                                             stop=(f is f_lo and k == HK - 1))
                m.then_inc(projected, 1)

            def project_pair(t, j, parts=(0, 1)):
                for e in parts:
                    if t == 0:
                        pe.wait_ge(lo_ready, HK * (2 * j + e + 1))
                    first = t == 0 and type(j) is int and j == 0
                    project(t, 2 * j + e, pair_ps[e], None if first else t * RESIDENT + 2 * j + e - 1)

            turn_sum(0)
            fuse(0)
            for t in range(TILES):
                pe.wait_ge(f_ready, HK * (t + 1))
                if t == 0:
                    project_pair(0, 0)
                with pe.Fori(1 if t == 0 else 0, PAIRS - 1) as j:
                    project_pair(t, j)
                if t == TILES - 1:
                    project_pair(t, PAIRS - 1)
                else:
                    project_pair(t, PAIRS - 1, (0,))
                    turn_sum(t + 1)
                    project_pair(t, PAIRS - 1, (1,))
                    fuse(t + 1)

            def phase2(c, slot):
                pe.wait_ge(lo_ready, HK * (c + 1))
                for t in range(TILES):
                    project(t, slot, phase2_ps[t], TILES * c + t - TILES + 1)

            for base in range(RESIDENT, CHUNKS - 1, RESIDENT):
                with pe.Fori(0, RESIDENT) as j:
                    phase2(base + j, j)
            phase2(CHUNKS - 1, 0)


_INS = ["r_user_rep", "r_indices", "L0_rec_item_embeddings", "L0_rec_W_fuse", "L0_rec_b_fuse", "L0_rec_W_proj",
        "L0_rec_b_proj"]


def kernel(**inputs):
    import numpy as np
    import concourse.bacc as bacc
    from concourse.bass_utils import run_bass_kernel_spmd

    nc = bacc.Bacc("TRN2", target_bir_lowering=False, num_devices=1)
    arrays, args = {}, []
    for name in _INS:
        a = np.ascontiguousarray(inputs[name])
        arrays[name] = a
        args.append(nc.dram_tensor(name, a.shape, mybir.dt.from_np(a.dtype), kind="ExternalInput").ap())
    shape = (inputs["r_user_rep"].shape[0], inputs["L0_rec_W_proj"].shape[1])
    args.append(nc.dram_tensor("logits", shape, F32, kind="ExternalOutput").ap())
    retrieval_scores(nc, *args)
    r = run_bass_kernel_spmd(nc, [arrays], core_ids=[0])
    return r.results[0]["logits"]
```

```python
from contextlib import ExitStack

import concourse.bass as bass
from concourse import mybir

P = 128
F32 = mybir.dt.float32
F32R = mybir.dt.float32r
I32 = mybir.dt.int32
ALU = mybir.AluOpType
ACT = mybir.ActivationFunctionType
AX_X = mybir.AxisListType.X

ACC_SLOTS = 5
LAPS = 2
TURN = LAPS * ACC_SLOTS
MIN_TURNS = 2
CHUNK = 500
RESIDENT = 8
EARLY = 3
AHEAD = 2
ROUND_F32 = float(2 ** 23)


def retrieval_scores(nc, user, indices, table, w_fuse, b_fuse, w_proj, b_proj, out):
    B, H = user.shape
    K = indices.shape[1]
    V = table.shape[0]
    TILES = B // P
    HK = H // P
    CHUNKS = V // CHUNK
    LAST = V - 1
    PAD = (K + 7) // 8 * 8
    PAIRS = RESIDENT // 2
    PHASE1 = TILES * RESIDENT
    assert B % P == 0 and H % P == 0 and V % CHUNK == 0 and K % TURN == 0 and TILES == 4 and HK == 4
    assert RESIDENT % 2 == 0 and (CHUNKS - 1) % RESIDENT == 0 and CHUNKS > 2 * RESIDENT

    idx_dram = indices.rearrange("(t p) k -> p t k", p=P)
    user_dram = user.rearrange("(t p) h -> p t h", p=P)
    wf_dram = w_fuse.rearrange("(s k p) n -> s p k n", s=2, p=P)
    bf_dram = b_fuse.rearrange("(k p) -> p k", p=P)
    wp_dram = w_proj.rearrange("(k p) v -> k p v", p=P)
    bp_dram = b_proj.rearrange("(a v) -> a v", a=1)
    out_dram = out.rearrange("(t p) v -> t p v", p=P)

    with ExitStack() as ctx:
        def sb(name, shape, dt=F32):
            return ctx.enter_context(nc.sbuf_tensor(name, shape, dt))

        def sem(name):
            return ctx.enter_context(nc.semaphore(name))

        w_hi = sb("w_hi", [P, RESIDENT, HK, CHUNK], F32R)
        w_lo = sb("w_lo", [P, RESIDENT, HK, CHUNK], F32R)
        w_raw = sb("w_raw", [P, 2, HK, CHUNK])
        f_hi = sb("f_hi", [P, TILES, HK, P], F32R)
        f_lo = sb("f_lo", [P, TILES, HK, P], F32R)
        acc = sb("acc", [P, 2, ACC_SLOTS, H])
        early = sb("early", [P, 2, HK, 512])
        user_t = early[:, 0, :, 0:B]
        wf_user = early[:, 1, :, 0:H]
        bias = early[:, :, :, :].rearrange("p a k n -> p (a k) n")
        user_sb = acc[:, 1, 0:TILES, :]
        wf_ret = sb("wf_ret", [P, HK, H])
        ret_t = sb("ret_t", [P, HK, P])
        bias_rows = ret_t[0:RESIDENT, :, :].rearrange("c k n -> c (k n)")[:, 0:CHUNK]
        last_row = sb("last_row", [P, H])
        bf_col = sb("bf_col", [P, HK])
        out_sb = sb("out_sb", [P, TILES, CHUNK])
        key = out_sb[:, 0, 0:TILES * K].rearrange("p (t k) -> p t k", k=K)
        flags = out_sb[:, 1, 0:TILES * K].rearrange("p (t k) -> p t k", k=K)
        key_left = out_sb[:, 2, 0:2 * K].rearrange("p (a k) -> p a k", k=K)
        ones_row = out_sb[0:1, 3, 0:P]
        ident = sb("ident", [P, P])
        idx = sb("idx", [P, TILES, K], I32)
        key_sorted = sb("key_sorted", [P, PAD])
        rows = sb("rows", [P, TILES, PAD], I32)
        lap_rows = sb("lap_rows", [P, LAPS, ACC_SLOTS], I32)
        n_inner = sb("n_inner", [P, TILES])
        turns_f = sb("turns_f", [1, TILES])
        turns_i = sb("turns_i", [1, TILES], I32)
        n_left = sb("n_left", [P, TILES])

        banks = [ctx.enter_context(nc.psum_tensor(f"bank{i}", [P, 512], F32)) for i in range(8)]
        fused_ps = banks[0:HK]
        tr_ps = banks[4]
        pair_ps = banks[5:7]
        small_ps = banks[7]
        phase2_ps = fused_ps

        idx_landed = sem("idx_landed")
        user_landed = sem("user_landed")
        wf_user_landed = sem("wf_user_landed")
        wf_ret_landed = sem("wf_ret_landed")
        last_landed = sem("last_landed")
        bf_landed = sem("bf_landed")
        w_landed = [[sem(f"w_landed{e}_{k}") for k in range(HK)] for e in range(2)]
        bias_rows_landed = sem("bias_rows_landed")
        bias_spread = sem("bias_spread")
        bias_ready = sem("bias_ready")
        bias_landed = sem("bias_landed")
        out_stored = [sem(f"out_stored{t}") for t in range(TILES)]
        gathered = [[sem(f"gathered{t}_{s}") for s in range(ACC_SLOTS)] for t in range(TILES)]
        lap_rows_set = [sem(f"lap_rows_set{t}") for t in range(TILES)]
        sum_landed = sem("sum_landed")
        pool_const = sem("pool_const")
        ident_ready = sem("ident_ready")
        ones_ready = sem("ones_ready")
        dve_step = sem("dve_step")
        rows_ready = sem("rows_ready")
        counted = sem("counted")
        counts_moved = sem("counts_moved")
        turns_ready = sem("turns_ready")
        turns_spread = sem("turns_spread")
        user_turned = sem("user_turned")
        user_t_ready = sem("user_t_ready")
        user_fused = sem("user_fused")
        summed = sem("summed")
        ret_turned = sem("ret_turned")
        ret_ready = sem("ret_ready")
        fused = sem("fused")
        f_hi_ready = sem("f_hi_ready")
        f_ready = sem("f_ready")
        hi_ready = sem("hi_ready")
        lo_ready = sem("lo_ready")
        projected = sem("projected")
        evacuated = sem("evacuated")

        def out_slot(t, e):
            return 2 * (t % 2) + e

        def phase2_all(engine, ahead, body):
            step = ahead // 2
            for base in range(PAIRS, CHUNKS // 2, PAIRS):
                for a, b, d in ((0, PAIRS - step, step), (PAIRS - step, PAIRS, step - PAIRS)):
                    inside = min(b, (CHUNKS - 1) // 2 - step - base)
                    if inside > a:
                        with engine.Fori(a, inside) as j:
                            for e in range(2):
                                body(base + j, e, j, j + d)
                    for j in range(max(a, inside), b):
                        for e in range(2):
                            body(base + j, e, j, j + d if 2 * (base + j) + e + ahead < CHUNKS else None)
            body(CHUNKS // 2, 0, 0, None)

        block = ctx.enter_context(nc.Block())

        @block.sync
        def _(sp):
            def load_unit(pair, e, k, wait=True):
                if wait:
                    sp.wait_ge(lo_ready, pair * (2 * HK) + (e - 2) * HK + k + 1)
                sp.dma_start(w_raw[:, e, k, :], wp_dram[k, :, bass.ds((2 * pair + e) * CHUNK, CHUNK)])\
                  .then_inc(w_landed[e][k], 16)

            def load_bias(c, slot):
                sp.dma_start(bias[:, bass.ds(slot, 1), 0:CHUNK],
                             bp_dram[:, bass.ds(c * CHUNK, CHUNK)].unsqueeze(1).to_broadcast([P, 1, CHUNK]))\
                  .then_inc(bias_landed, 16)

            def store(t, c, group, slot):
                sp.wait_ge(evacuated, group + 1)
                sp.dma_start(out_dram[t, :, bass.ds(c * CHUNK, CHUNK)], out_sb[:, slot, :])\
                  .then_inc(out_stored[slot], 16)

            sp.dma_start(idx[:], idx_dram).then_inc(idx_landed, 16)
            for c in range(2):
                for k in range(HK):
                    load_unit(0, c, k, wait=False)
            sp.dma_start(bias_rows, b_proj[0:RESIDENT * CHUNK].rearrange("(c n) -> c n", n=CHUNK))\
              .then_inc(bias_rows_landed, 16)
            sp.dma_start(last_row[:], table[LAST:V, :].to_broadcast([P, H])).then_inc(last_landed, 16)
            sp.dma_start(wf_ret[:], wf_dram[1]).then_inc(wf_ret_landed, 16)
            for c in range(2, EARLY + 2):
                if c == EARLY:
                    sp.wait_ge(summed, 1)
                for k in range(HK):
                    load_unit(c // 2, c % 2, k)

            for j in range(RESIDENT):
                store(0, j, j, out_slot(0, j % 2))
                c = j + EARLY + 2
                if c < RESIDENT + 2:
                    for k in range(HK):
                        load_unit(c // 2, c % 2, k)
            for t in range(1, TILES - 1):
                with sp.Fori(0, PAIRS) as j:
                    for e in range(2):
                        store(t, 2 * j + e, t * RESIDENT + 2 * j + e, out_slot(t, e))
            t = TILES - 1
            for j in range(RESIDENT):
                store(t, j, t * RESIDENT + j, out_slot(t, j % 2))
                load_unit(PAIRS + 1, j // HK, j % HK)
                if j < 2 + AHEAD:
                    if j:
                        sp.wait_ge(bias_landed, 16 * j)
                    load_bias(RESIDENT + j, j)

            def phase2(pair, e, ring, ring_ahead):
                c = 2 * pair + e
                for t in range(TILES):
                    store(t, c, TILES * c + t, t)
                    if ring_ahead is not None:
                        load_unit(pair + 1 + AHEAD // 2, e, t)
                        if t == 0:
                            sp.wait_ge(bias_landed, 16 * (c + AHEAD + 2 - RESIDENT))
                            load_bias(c + AHEAD + 2, 2 * ring_ahead + e)

            phase2_all(sp, AHEAD + 2, phase2)
            for t in range(TILES):
                sp.wait_ge(out_stored[t], 16 * CHUNKS)

        @block.gpsimd
        def _(pool):
            nc.gpsimd.memset(ident[:], 0.0).then_inc(pool_const, 1)
            nc.gpsimd.memset(ones_row, 1.0).then_inc(ones_ready, 1)
            pool.wait_ge(pool_const, 1)
            nc.gpsimd.affine_select(out=ident[:], in_=ident[:], compare_op=ALU.not_equal, fill=1.0, base=0,
                                    pattern=[[-1, P]], channel_multiplier=1).then_inc(ident_ready, 1)

            def gather(t, s, column, **how):
                return nc.gpsimd.indirect_dma_start(
                    out=acc[:, t % 2, s, :], out_offset=None, in_=table,
                    in_offset=bass.IndirectOffsetOnAxis(ap=column, axis=0), **how)

            for t in range(TILES):
                pool.wait_ge(rows_ready, 1 if t == 0 else PAD // 8 + t)
                if t == 1:
                    pool.wait_ge(user_turned, HK)
                if t >= 2:
                    pool.wait_ge(ret_turned, t - 1)
                for s in range(ACC_SLOTS):
                    gather(t, s, rows[:, t, s:s + 1]).then_inc(gathered[t][s], 16)
                if t == 0:
                    pool.wait_ge(rows_ready, 2)
                for s in range(ACC_SLOTS):
                    pool.wait_ge(gathered[t][s], 16)
                    gather(t, s, rows[:, t, ACC_SLOTS + s:ACC_SLOTS + s + 1], compute_op=ALU.add)\
                        .then_inc(gathered[t][s], 16)
                if t == 0:
                    pool.wait_ge(turns_ready, 1)
                    pool.wait_ge(rows_ready, PAD // 8)
                turns = pool.value_load(turns_i[0:1, t:t + 1], min_val=MIN_TURNS, max_val=K // TURN)
                with pool.Fori(1, turns) as turn:
                    for lap in range(LAPS):
                        first = (turn * LAPS + lap) * ACC_SLOTS
                        nc.gpsimd.tensor_copy(lap_rows[:, lap, :], rows[:, t, bass.ds(first, ACC_SLOTS)])\
                          .then_inc(lap_rows_set[t], 1)
                        pool.wait_ge(lap_rows_set[t], turn * LAPS + (lap + 1 - LAPS))
                        for s in range(ACC_SLOTS):
                            pool.wait_ge(gathered[t][s], turn * (16 * LAPS) + 16 * lap)
                            pool.sem_inc(sum_landed, 1)
                            gather(t, s, lap_rows[:, lap, s:s + 1], compute_op=ALU.add).then_inc(gathered[t][s], 16)

        @block.scalar
        def _(act):
            def split_hi(pair, e, slot, free=None):
                for k in range(HK):
                    act.wait_ge(w_landed[e][k], pair * 16 + 16)
                    if free is not None and k == 0:
                        act.wait_ge(projected, free)
                    nc.scalar.copy(w_hi[:, bass.ds(slot, 1), k, :], w_raw[:, e, k:k + 1, :]).then_inc(hi_ready, 1)

            act.dma_start(user_sb, user_dram).then_inc(user_landed, 16)
            act.dma_start(wf_user, wf_dram[0]).then_inc(wf_user_landed, 16)
            with nc.allow_non_contiguous_dma(reason="512 words, once"):
                act.dma_start(bf_col[:], bf_dram).then_inc(bf_landed, 16)

            for k in range(HK):
                act.wait_ge(user_turned, k + 1)
                nc.scalar.copy(user_t[:, k, :], banks[k][:, :]).then_inc(user_t_ready, 1)
            for c in range(EARLY):
                split_hi(c // 2, c % 2, c)
            for c in range(RESIDENT):
                act.wait_ge(bias_spread, c + 1)
                nc.scalar.copy(bias[:, c, 0:CHUNK], pair_ps[c % 2][:, 0:CHUNK]).then_inc(bias_ready, 1)

            def fuse(t):
                act.wait_ge(ret_turned, t + 1)
                act.wait_ge(fused, HK * t) if t else act.wait_ge(bias_spread, RESIDENT)
                nc.scalar.mul(ret_t[:], tr_ps[:, :].rearrange("p (k n) -> p k n", k=HK), 1.0 / K)\
                  .then_inc(ret_ready, 1)
                if t == 0:
                    act.wait_ge(bf_landed, 16)
                for k in range(HK):
                    act.wait_ge(fused, HK * t + k + 1)
                    nc.scalar.activation(f_hi[:, t, k, :], fused_ps[k][:, t * P:(t + 1) * P], ACT.Identity,
                                         bias=bf_col[:, k:k + 1]).then_inc(f_hi_ready, 1)

            fuse(0)
            for c in range(EARLY, RESIDENT):
                split_hi(c // 2, c % 2, c)
            for t in range(1, TILES):
                fuse(t)
            with act.Fori(0, PAIRS) as j:
                for e in range(2):
                    split_hi(j + PAIRS, e, 2 * j + e, 2 * j + (TILES - 1) * RESIDENT + e + 1)
            with act.Fori(0, PAIRS) as j:
                for e in range(2):
                    split_hi(j + 2 * PAIRS, e, 2 * j + e, j * (2 * TILES) + PHASE1 + TILES * (e + 1))
            split_hi(CHUNKS // 2, 0, 0, PHASE1 + TILES * RESIDENT + TILES)

        @block.vector
        def _(dve):
            steps = [0]

            def then(instruction):
                steps[0] += 1
                instruction.then_inc(dve_step, 1)
                dve.wait_ge(dve_step, steps[0])

            def split_lo(e, slot, k, count):
                dve.wait_ge(hi_ready, count)
                nc.vector.tensor_tensor(w_lo[:, bass.ds(slot, 1), k, :], w_raw[:, e, k:k + 1, :],
                                        w_hi[:, bass.ds(slot, 1), k, :].bitcast(F32), ALU.subtract)\
                  .then_inc(lo_ready, 1)

            def sort(t):
                src = key[:, t, :]
                for n in range(PAD // 8):
                    top = key_sorted[:, 8 * n:8 * n + 8]
                    then(nc.vector.max(top, src))
                    if t == 0:
                        nc.vector.tensor_scalar(rows[:, t, 8 * n:8 * n + 8], top, -1.0, float(LAST),
                                                ALU.mult, ALU.add).then_inc(rows_ready, 1)
                    if n < PAD // 8 - 1:
                        rest = key_left[:, n % 2, :]
                        then(nc.vector.match_replace(out=rest, in_to_replace=top, in_values=src, imm_value=0.0))
                        src = rest
                if t:
                    nc.vector.tensor_scalar(rows[:, t, :], key_sorted[:], -1.0, float(LAST), ALU.mult, ALU.add)\
                      .then_inc(rows_ready, 1)
                dve.wait_ge(rows_ready, PAD // 8 + t)

            dve.wait_ge(idx_landed, 16)
            then(nc.vector.tensor_scalar(key, idx[:], 0.0, float(V), ALU.is_lt, ALU.mult))
            then(nc.vector.tensor_tensor(key, key, idx[:], ALU.add))
            then(nc.vector.tensor_scalar(key, key, 0.0, float(LAST), ALU.max, ALU.min))
            then(nc.vector.tensor_scalar(key, key, -1.0, float(LAST), ALU.mult, ALU.add))
            sort(0)
            then(nc.vector.tensor_scalar(flags, key, 0.0, None, ALU.is_gt))
            nc.vector.tensor_reduce(n_inner[:], flags, AX_X, ALU.add).then_inc(counted, 1)
            dve.wait_ge(counts_moved, 1)
            then(nc.vector.tensor_reduce(turns_f[:], small_ps[0:1, :].rearrange("a (t p) -> a t p", p=P), AX_X, ALU.max))
            then(nc.vector.tensor_scalar(turns_f[:], turns_f[:], float(TURN * MIN_TURNS), 1.0 / TURN,
                                         ALU.max, ALU.mult))
            then(nc.vector.tensor_scalar(turns_f[:], turns_f[:], 0.5 - 0.5 / TURN, ROUND_F32, ALU.add, ALU.add))
            then(nc.vector.tensor_scalar(turns_f[:], turns_f[:], ROUND_F32, None, ALU.subtract))
            nc.vector.tensor_copy(turns_i[:], turns_f[:]).then_inc(turns_ready, 1)
            dve.wait_ge(turns_spread, 1)
            then(nc.vector.tensor_scalar(n_left[:], small_ps[:, 0:TILES], -float(TURN), float(K),
                                         ALU.mult, ALU.add))
            def split_chunk(c):
                for k in range(HK):
                    split_lo(c % 2, c, k, HK * c + k + 1)

            for t in range(1, TILES):
                split_chunk(t - 1)
                sort(t)

            def sum_half(t, half):
                if half == 0:
                    turns = dve.value_load(turns_i[0:1, t:t + 1], min_val=MIN_TURNS, max_val=K // TURN)
                    for s in range(ACC_SLOTS):
                        dve.wait_ge(gathered[t][s], turns * (16 * LAPS))
                cols = slice(half * H // 2, (half + 1) * H // 2)
                then(nc.vector.tensor_reduce(small_ps[:, cols],
                                             acc[:, t % 2, :, cols].rearrange("p s h -> p h s"), AX_X, ALU.add))

            def add_last(t):
                if t == 0:
                    dve.wait_ge(last_landed, 16)
                nc.vector.scalar_tensor_tensor(acc[:, t % 2, 0, :], last_row[:], n_left[:, t:t + 1],
                                               small_ps[:, 0:H], ALU.mult, ALU.add).then_inc(summed, 1)

            def fused_lo(t):
                if t == 0:
                    dve.wait_ge(bf_landed, 16)
                for k in range(HK):
                    dve.wait_ge(f_hi_ready, HK * t + k + 1)
                    nc.vector.scalar_tensor_tensor(f_lo[:, t, k, :], fused_ps[k][:, t * P:(t + 1) * P],
                                                   bf_col[:, k:k + 1], f_hi[:, t, k, :].bitcast(F32),
                                                   ALU.add, ALU.subtract).then_inc(f_ready, 1)

            def evacuate(ps, group, slot, bias_slot, stored=None):
                dve.wait_ge(projected, group + 1)
                if stored is not None:
                    dve.wait_ge(out_stored[slot], stored)
                nc.vector.tensor_tensor(out_sb[:, slot:slot + 1, :], ps[:, 0:CHUNK].unsqueeze(1),
                                        bias[:, bass.ds(bias_slot, 1), 0:CHUNK], ALU.add).then_inc(evacuated, 1)

            def evacuate_pair(t, j, parts=(0, 1)):
                for e in parts:
                    first = t < 2 and type(j) is int and j == 0
                    evacuate(pair_ps[e], t * RESIDENT + 2 * j + e, out_slot(t, e), 2 * j + e,
                             None if first else 16 * (t // 2 * PAIRS + j))

            sum_half(0, 0)
            sum_half(0, 1)
            add_last(0)
            fused_lo(0)
            dve.wait_ge(bias_ready, RESIDENT)
            for t in range(TILES - 1):
                if t == 0:
                    for j in range(PAIRS - 1):
                        for e in range(2):
                            if 2 * j + e < RESIDENT - EARLY:
                                evacuate_pair(0, j, (e,))
                                split_chunk(2 * j + e + EARLY)
                if t == 1:
                    evacuate_pair(t, 0)
                if t >= 1:
                    with dve.Fori(1 if t == 1 else 0, PAIRS - 2) as j:
                        evacuate_pair(t, j)
                    evacuate_pair(t, PAIRS - 2, (0,))
                sum_half(t + 1, 0)
                evacuate_pair(t, PAIRS - 2, (1,))
                sum_half(t + 1, 1)
                add_last(t + 1)
                evacuate_pair(t, PAIRS - 1)
                fused_lo(t + 1)
            for j in range(RESIDENT):
                evacuate_pair(TILES - 1, j // 2, (j % 2,))
                split_lo(j // HK, j // HK, j % HK, HK * RESIDENT + j + 1)

            def phase2(pair, e, ring, ring_ahead):
                c = 2 * pair + e
                dve.wait_ge(bias_landed, 16 * (c - RESIDENT + 1))
                for t in range(TILES):
                    evacuate(phase2_ps[t], TILES * c + t, t, 2 * ring + e, 16 * c)
                    if ring_ahead is not None:
                        split_lo(e, 2 * ring_ahead + e, t, HK * (c + AHEAD) + t + 1)

            phase2_all(dve, AHEAD, phase2)

        @block.tensor
        def _(pe):
            pe.wait_ge(ident_ready, 1)
            pe.wait_ge(user_landed, 16)
            for k in range(HK):
                for t in range(TILES):
                    m = nc.tensor.transpose(banks[k][:, t * P:(t + 1) * P], user_sb[:, t, k * P:(k + 1) * P], ident[:])
                m.then_inc(user_turned, 1)

            pe.wait_ge(counted, 1)
            for t in range(TILES):
                m = nc.tensor.matmul(small_ps[0:1, t * P:(t + 1) * P], n_inner[:, t:t + 1], ident[:],
                                     start=True, stop=True)
            m.then_inc(counts_moved, 1)
            pe.wait_ge(ones_ready, 1)
            pe.wait_ge(turns_ready, 1)
            nc.tensor.matmul(small_ps[:, 0:TILES], ones_row, turns_f[:], start=True, stop=True).then_inc(turns_spread, 1)

            pe.wait_ge(user_t_ready, HK)
            pe.wait_ge(wf_user_landed, 16)
            for n in range(HK):
                for k in range(HK):
                    m = nc.tensor.matmul(fused_ps[n][:, :], wf_user[:, k, n * P:(n + 1) * P], user_t[:, k, :],
                                         start=(k == 0), stop=(k == HK - 1))
                m.then_inc(user_fused, 1)

            pe.wait_ge(bias_rows_landed, 16)
            for c in range(RESIDENT):
                if c >= 2:
                    pe.wait_ge(bias_ready, c - 1)
                nc.tensor.matmul(pair_ps[c % 2][:, 0:CHUNK], ident[0:RESIDENT, c:c + 1].to_broadcast([RESIDENT, P]),
                                 bias_rows, start=True, stop=True).then_inc(bias_spread, 1)

            def turn_sum(t):
                pe.wait_ge(summed, t + 1)
                if t:
                    pe.wait_ge(ret_ready, t)
                for k in range(HK):
                    m = nc.tensor.transpose(tr_ps[:, k * P:(k + 1) * P], acc[:, t % 2, 0, k * P:(k + 1) * P], ident[:])
                m.then_inc(ret_turned, 1)

            def fuse(t):
                pe.wait_ge(ret_ready, t + 1)
                if t == 0:
                    pe.wait_ge(wf_ret_landed, 16)
                for n in range(HK):
                    for k in range(HK):
                        m = nc.tensor.matmul(fused_ps[n][:, t * P:(t + 1) * P], wf_ret[:, k, n * P:(n + 1) * P],
                                             ret_t[:, k, :], start=False, stop=(k == HK - 1), skip_group_check=True)
                    m.then_inc(fused, 1)

            def project(t, slot, ps, free=None):
                if free is not None:
                    pe.wait_ge(evacuated, free)
                for k in range(HK):
                    hi, lo = w_hi[:, bass.ds(slot, 1), k, :], w_lo[:, bass.ds(slot, 1), k, :]
                    for f, w, first in ((f_hi, hi, k == 0), (f_hi, lo, False), (f_lo, hi, False)):
                        m = nc.tensor.matmul(ps[:, 0:CHUNK].unsqueeze(1), f[:, t, k, :], w, start=first,
                                             stop=(f is f_lo and k == HK - 1))
                m.then_inc(projected, 1)

            def project_pair(t, j, parts=(0, 1)):
                for e in parts:
                    if t == 0:
                        pe.wait_ge(lo_ready, HK * (2 * j + e + 1))
                        if type(j) is int and j == 0:
                            pe.wait_ge(bias_ready, RESIDENT - 1 + e)
                    first = t == 0 and type(j) is int and j == 0
                    project(t, 2 * j + e, pair_ps[e], None if first else t * RESIDENT + 2 * j + e - 1)

            turn_sum(0)
            fuse(0)
            for t in range(TILES):
                pe.wait_ge(f_ready, HK * (t + 1))
                if t == 0:
                    project_pair(0, 0)
                with pe.Fori(1 if t == 0 else 0, PAIRS - 1) as j:
                    project_pair(t, j)
                if t == TILES - 1:
                    project_pair(t, PAIRS - 1)
                else:
                    project_pair(t, PAIRS - 1, (0,))
                    turn_sum(t + 1)
                    project_pair(t, PAIRS - 1, (1,))
                    fuse(t + 1)

            def phase2(c, slot):
                pe.wait_ge(lo_ready, HK * (c + 1))
                for t in range(TILES):
                    project(t, slot, phase2_ps[t], TILES * c + t - TILES + 1)

            for base in range(RESIDENT, CHUNKS - 1, RESIDENT):
                with pe.Fori(0, RESIDENT) as j:
                    phase2(base + j, j)
            phase2(CHUNKS - 1, 0)


_INS = ["r_user_rep", "r_indices", "L0_rec_item_embeddings", "L0_rec_W_fuse", "L0_rec_b_fuse", "L0_rec_W_proj",
        "L0_rec_b_proj"]


def kernel(**inputs):
    import numpy as np
    import concourse.bacc as bacc
    from concourse.bass_utils import run_bass_kernel_spmd

    nc = bacc.Bacc("TRN2", target_bir_lowering=False, num_devices=1, dynamic_dma_scratch_size=8192)
    arrays, args = {}, []
    for name in _INS:
        a = np.ascontiguousarray(inputs[name])
        arrays[name] = a
        args.append(nc.dram_tensor(name, a.shape, mybir.dt.from_np(a.dtype), kind="ExternalInput").ap())
    shape = (inputs["r_user_rep"].shape[0], inputs["L0_rec_W_proj"].shape[1])
    args.append(nc.dram_tensor("logits", shape, F32, kind="ExternalOutput").ap())
    retrieval_scores(nc, *args)
    r = run_bass_kernel_spmd(nc, [arrays], core_ids=[0])
    return r.results[0]["logits"]
```

```python
from contextlib import ExitStack

import concourse.bass as bass
from concourse import mybir

P = 128
F32 = mybir.dt.float32
F32R = mybir.dt.float32r
I32 = mybir.dt.int32
ALU = mybir.AluOpType
ACT = mybir.ActivationFunctionType
AX_X = mybir.AxisListType.X

ACC_SLOTS = 5
LAPS = 2
TURN = LAPS * ACC_SLOTS
MIN_TURNS = 2
CHUNK = 500
RESIDENT = 8
EARLY = 3
LATE = 6
AHEAD = 2
ROUND_F32 = float(2 ** 23)


def retrieval_scores(nc, user, indices, table, w_fuse, b_fuse, w_proj, b_proj, out):
    B, H = user.shape
    K = indices.shape[1]
    V = table.shape[0]
    TILES = B // P
    HK = H // P
    CHUNKS = V // CHUNK
    LAST = V - 1
    PAD = (K + 7) // 8 * 8
    PAIRS = RESIDENT // 2
    PHASE1 = TILES * RESIDENT
    assert B % P == 0 and H % P == 0 and V % CHUNK == 0 and K % TURN == 0 and TILES == 4 and HK == 4
    assert RESIDENT % 2 == 0 and (CHUNKS - 1) % RESIDENT == 0 and CHUNKS > 2 * RESIDENT
    assert LATE == RESIDENT - 2 == TILES + 2 and LATE - EARLY <= TILES

    idx_dram = indices.rearrange("(t p) k -> p t k", p=P)
    user_dram = user.rearrange("(t p) h -> p t h", p=P)
    wf_dram = w_fuse.rearrange("(s k p) n -> s p k n", s=2, p=P)
    bf_dram = b_fuse.rearrange("(k p) -> p k", p=P)
    wp_dram = w_proj.rearrange("(k p) v -> k p v", p=P)
    bp_dram = b_proj.rearrange("(a v) -> a v", a=1)
    out_dram = out.rearrange("(t p) v -> t p v", p=P)

    with ExitStack() as ctx:
        def sb(name, shape, dt=F32):
            return ctx.enter_context(nc.sbuf_tensor(name, shape, dt))

        def sem(name):
            return ctx.enter_context(nc.semaphore(name))

        w_hi = sb("w_hi", [P, RESIDENT, HK, CHUNK], F32R)
        w_lo = sb("w_lo", [P, RESIDENT, HK, CHUNK], F32R)
        w_raw = sb("w_raw", [P, 2, HK, CHUNK])
        f_hi = sb("f_hi", [P, TILES, HK, P], F32R)
        f_lo = sb("f_lo", [P, TILES, HK, P], F32R)
        acc = sb("acc", [P, 2, ACC_SLOTS, H])
        early = sb("early", [P, 2, HK, 512])
        user_t = early[:, 0, :, 0:B]
        wf_user = early[:, 1, :, 0:H]
        bias = early[:, :, :, :].rearrange("p a k n -> p (a k) n")
        bias_rows = bias[0:RESIDENT, RESIDENT - 1, 0:CHUNK]
        user_sb = acc[:, 1, 0:TILES, :]
        wf_ret = sb("wf_ret", [P, HK, H])
        ret_t = sb("ret_t", [P, HK, P])
        last_row = sb("last_row", [P, H])
        bf_col = sb("bf_col", [P, HK])
        out_sb = sb("out_sb", [P, TILES, CHUNK])
        key = out_sb[:, 0, 0:TILES * K].rearrange("p (t k) -> p t k", k=K)
        flags = out_sb[:, 1, 0:TILES * K].rearrange("p (t k) -> p t k", k=K)
        key_left = out_sb[:, 2, 0:2 * K].rearrange("p (a k) -> p a k", k=K)
        ones_row = out_sb[0:1, 3, 0:P]
        ident = sb("ident", [P, P])
        pool_mark = sb("pool_mark", [1, 1])
        idx = sb("idx", [P, TILES, K], I32)
        key_sorted = sb("key_sorted", [P, PAD])
        rows = sb("rows", [P, TILES, PAD], I32)
        lap_rows = sb("lap_rows", [P, LAPS, ACC_SLOTS], I32)
        n_inner = sb("n_inner", [P, TILES])
        turns_f = sb("turns_f", [1, TILES])
        turns_i = sb("turns_i", [1, TILES], I32)
        n_left = sb("n_left", [P, TILES])

        banks = [ctx.enter_context(nc.psum_tensor(f"bank{i}", [P, 512], F32)) for i in range(8)]
        fused_ps = banks[0:HK]
        tr_ps = banks[4]
        pair_ps = banks[5:7]
        small_ps = banks[7]
        phase2_ps = fused_ps

        idx_landed = sem("idx_landed")
        user_landed = sem("user_landed")
        wf_user_landed = sem("wf_user_landed")
        wf_ret_landed = sem("wf_ret_landed")
        last_landed = sem("last_landed")
        last_spread = sem("last_spread")
        last_ready = sem("last_ready")
        bf_landed = sem("bf_landed")
        w_landed = [[sem(f"w_landed{e}_{k}") for k in range(HK)] for e in range(2)]
        bias_rows_landed = sem("bias_rows_landed")
        bias_spread = sem("bias_spread")
        bias_ready = sem("bias_ready")
        bias_landed = sem("bias_landed")
        out_stored = [sem(f"out_stored{t}") for t in range(TILES)]
        gathered = [[sem(f"gathered{t}_{s}") for s in range(ACC_SLOTS)] for t in range(TILES)]
        lap_rows_set = [sem(f"lap_rows_set{t}") for t in range(TILES)]
        sum_landed = sem("sum_landed")
        gathers_issued = sem("gathers_issued")
        pool_const = sem("pool_const")
        ident_ready = sem("ident_ready")
        ones_ready = sem("ones_ready")
        dve_step = sem("dve_step")
        rows_ready = sem("rows_ready")
        counted = sem("counted")
        counts_moved = sem("counts_moved")
        turns_ready = sem("turns_ready")
        turns_spread = sem("turns_spread")
        user_turned = sem("user_turned")
        user_t_ready = sem("user_t_ready")
        user_fused = sem("user_fused")
        summed = sem("summed")
        ret_turned = sem("ret_turned")
        ret_ready = sem("ret_ready")
        fused = sem("fused")
        f_hi_ready = sem("f_hi_ready")
        f_ready = sem("f_ready")
        hi_ready = sem("hi_ready")
        lo_ready = sem("lo_ready")
        projected = sem("projected")
        evacuated = sem("evacuated")

        def out_slot(t, c):
            if t == 0:
                return c % (RESIDENT - 1) % TILES
            return c % 2 if t % 2 == 0 else TILES - 1 - c % 2

        def stored_before(t, e):
            slot = e if t == TILES else out_slot(t, e)
            return sum(out_slot(u, c) == slot for u in range(t) for c in range(RESIDENT))

        def phase2_all(engine, ahead, body):
            step = ahead // 2
            for base in range(PAIRS, CHUNKS // 2, PAIRS):
                for a, b, d in ((0, PAIRS - step, step), (PAIRS - step, PAIRS, step - PAIRS)):
                    inside = min(b, (CHUNKS - 1) // 2 - step - base)
                    if inside > a:
                        with engine.Fori(a, inside) as j:
                            for e in range(2):
                                body(base + j, e, j, j + d)
                    for j in range(max(a, inside), b):
                        for e in range(2):
                            body(base + j, e, j, j + d if 2 * (base + j) + e + ahead < CHUNKS else None)
            body(CHUNKS // 2, 0, 0, None)

        def bias_ps(c):
            return pair_ps[c] if c < 2 else small_ps

        block = ctx.enter_context(nc.Block())

        @block.sync
        def _(sp):
            def load_unit(pair, e, k, wait=True):
                if wait:
                    sp.wait_ge(lo_ready, pair * (2 * HK) + (e - 2) * HK + k + 1)
                sp.dma_start(w_raw[:, e, k, :], wp_dram[k, :, bass.ds((2 * pair + e) * CHUNK, CHUNK)])\
                  .then_inc(w_landed[e][k], 16)

            def load_bias(c, slot):
                sp.dma_start(bias[:, bass.ds(slot, 1), 0:CHUNK],
                             bp_dram[:, bass.ds(c * CHUNK, CHUNK)].unsqueeze(1).to_broadcast([P, 1, CHUNK]))\
                  .then_inc(bias_landed, 16)

            def store(t, c, group, slot):
                sp.wait_ge(evacuated, group + 1)
                sp.dma_start(out_dram[t, :, bass.ds(c * CHUNK, CHUNK)], out_sb[:, slot, :])\
                  .then_inc(out_stored[slot], 16)

            def after_gather(lap, s):
                sp.wait_ge(gathered[0][s], 16 * (lap + 1))

            def load_wf_ret(k):
                sp.dma_start(wf_ret[:, k, :], wf_dram[1, :, k, :]).then_inc(wf_ret_landed, 16)

            sp.dma_start(idx[:], idx_dram).then_inc(idx_landed, 16)
            sp.dma_start(last_row[0:1, :], table[LAST:V, :]).then_inc(last_landed, 16)
            for k in range(HK):
                after_gather(0, k + 1)
                load_unit(0, 0, k, wait=False)
            for k in range(HK):
                after_gather(2 + k // 2, 2 * (k % 2))
                load_wf_ret(k)

            def load_chunk(c):
                for k in range(HK):
                    load_unit(c // 2, c % 2, k, wait=c >= 2)

            for c in range(1, LATE):
                if c == 2:
                    sp.wait_ge(user_fused, HK)
                    sp.dma_start(bias_rows, b_proj[0:RESIDENT * CHUNK].rearrange("(c n) -> c n", n=CHUNK))\
                      .then_inc(bias_rows_landed, 16)
                load_chunk(c)
            sp.wait_ge(gathers_issued, 2)
            for c in range(LATE, RESIDENT):
                store(0, c - LATE, c - LATE, out_slot(0, c - LATE))
                load_chunk(c)
            for c in range(RESIDENT - LATE, RESIDENT - 1):
                store(0, c, c, out_slot(0, c))
            store(1, 0, RESIDENT - 1, out_slot(1, 0))
            store(0, RESIDENT - 1, RESIDENT, out_slot(0, RESIDENT - 1))
            store(1, 1, RESIDENT + 1, out_slot(1, 1))

            def store_tile(t, a, b):
                with sp.Fori(a, b) as j:
                    for e in range(2):
                        store(t, 2 * j + e, t * RESIDENT + 2 * j + e, out_slot(t, e))

            store_tile(1, 1, PAIRS)
            store_tile(2, 0, PAIRS - 2)
            sp.wait_ge(gathers_issued, TILES)
            for c in range(RESIDENT, RESIDENT + 2):
                load_chunk(c)
            store_tile(2, PAIRS - 2, PAIRS)
            t = TILES - 1
            for j in range(RESIDENT):
                store(t, j, t * RESIDENT + j, out_slot(t, j))
                load_unit(PAIRS + 1, j // HK, j % HK)
                if j < 2 + AHEAD:
                    if j:
                        sp.wait_ge(bias_landed, 16 * j)
                    load_bias(RESIDENT + j, j)

            def phase2(pair, e, ring, ring_ahead):
                c = 2 * pair + e
                for t in range(TILES):
                    store(t, c, TILES * c + t, t)
                    if ring_ahead is not None:
                        load_unit(pair + 1 + AHEAD // 2, e, t)
                        if t == 0:
                            sp.wait_ge(bias_landed, 16 * (c + AHEAD + 2 - RESIDENT))
                            load_bias(c + AHEAD + 2, 2 * ring_ahead + e)

            phase2_all(sp, AHEAD + 2, phase2)
            for t in range(TILES):
                sp.wait_ge(out_stored[t], 16 * (CHUNKS - RESIDENT + stored_before(TILES, t)))

        @block.gpsimd
        def _(pool):
            nc.gpsimd.memset(ident[:], 0.0).then_inc(pool_const, 1)
            nc.gpsimd.memset(ones_row, 1.0).then_inc(ones_ready, 1)
            pool.wait_ge(pool_const, 1)
            nc.gpsimd.affine_select(out=ident[:], in_=ident[:], compare_op=ALU.not_equal, fill=1.0, base=0,
                                    pattern=[[-1, P]], channel_multiplier=1).then_inc(ident_ready, 1)

            def gather(t, s, column, **how):
                return nc.gpsimd.indirect_dma_start(
                    out=acc[:, t % 2, s, :], out_offset=None, in_=table,
                    in_offset=bass.IndirectOffsetOnAxis(ap=column, axis=0), **how)

            for t in range(TILES):
                pool.wait_ge(rows_ready, 1 if t == 0 else PAD // 8 + t)
                if t == 1:
                    pool.wait_ge(user_turned, HK)
                if t >= 2:
                    pool.wait_ge(ret_turned, t - 1)
                for s in range(ACC_SLOTS):
                    gather(t, s, rows[:, t, s:s + 1]).then_inc(gathered[t][s], 16)
                if t == 0:
                    pool.wait_ge(rows_ready, 2)
                for s in range(ACC_SLOTS):
                    pool.wait_ge(gathered[t][s], 16)
                    gather(t, s, rows[:, t, ACC_SLOTS + s:ACC_SLOTS + s + 1], compute_op=ALU.add)\
                        .then_inc(gathered[t][s], 16)
                if t == 0:
                    pool.wait_ge(turns_ready, 1)
                    pool.wait_ge(rows_ready, PAD // 8)
                turns = pool.value_load(turns_i[0:1, t:t + 1], min_val=MIN_TURNS, max_val=K // TURN)
                with pool.Fori(1, turns) as turn:
                    for lap in range(LAPS):
                        first = (turn * LAPS + lap) * ACC_SLOTS
                        nc.gpsimd.tensor_copy(lap_rows[:, lap, :], rows[:, t, bass.ds(first, ACC_SLOTS)])\
                          .then_inc(lap_rows_set[t], 1)
                        pool.wait_ge(lap_rows_set[t], turn * LAPS + (lap + 1 - LAPS))
                        for s in range(ACC_SLOTS):
                            pool.wait_ge(gathered[t][s], turn * (16 * LAPS) + 16 * lap)
                            pool.sem_inc(sum_landed, 1)
                            gather(t, s, lap_rows[:, lap, s:s + 1], compute_op=ALU.add).then_inc(gathered[t][s], 16)
                nc.gpsimd.memset(pool_mark[:], 0.0).then_inc(gathers_issued, 1)

        @block.scalar
        def _(act):
            def split_hi(pair, e, slot, free=None, units=range(HK)):
                for k in units:
                    act.wait_ge(w_landed[e][k], pair * 16 + 16)
                    if free is not None and k == 0:
                        act.wait_ge(projected, free)
                    nc.scalar.copy(w_hi[:, bass.ds(slot, 1), k, :], w_raw[:, e, k:k + 1, :]).then_inc(hi_ready, 1)

            act.dma_start(user_sb, user_dram).then_inc(user_landed, 16)
            act.dma_start(wf_user, wf_dram[0]).then_inc(wf_user_landed, 16)
            with nc.allow_non_contiguous_dma(reason="512 words, once"):
                act.dma_start(bf_col[:], bf_dram).then_inc(bf_landed, 16)

            for k in range(HK):
                act.wait_ge(user_turned, k + 1)
                nc.scalar.copy(user_t[:, k, :], banks[k][:, :]).then_inc(user_t_ready, 1)

            def spread_bias(c):
                act.wait_ge(bias_spread, c + 1)
                nc.scalar.copy(bias[:, c, 0:CHUNK], bias_ps(c)[:, 0:CHUNK]).then_inc(bias_ready, 1)

            def mean(t):
                act.wait_ge(ret_turned, t + 1)
                if t:
                    act.wait_ge(fused, HK * t)
                nc.scalar.mul(ret_t[:], tr_ps[:, :].rearrange("p (k n) -> p k n", k=HK), 1.0 / K)\
                  .then_inc(ret_ready, 1)

            def fused_hi(t, k):
                act.wait_ge(fused, HK * t + k + 1)
                nc.scalar.activation(f_hi[:, t, k, :], fused_ps[k][:, t * P:(t + 1) * P], ACT.Identity,
                                     bias=bf_col[:, k:k + 1]).then_inc(f_hi_ready, 1)

            act.wait_ge(last_spread, 1)
            nc.scalar.copy(last_row[:], pair_ps[0][:, :]).then_inc(last_ready, 1)
            split_hi(0, 0, 0)
            mean(0)
            act.wait_ge(bf_landed, 16)
            for k in range(HK):
                split_hi(0, 1, 1, units=(k,))
                fused_hi(0, k)
            for c in range(2):
                spread_bias(c)
            for c in range(2, LATE):
                split_hi(c // 2, c % 2, c)
                spread_bias(c)
            spread_bias(LATE)
            mean(1)
            split_hi(LATE // 2, 0, LATE)
            for k in range(HK):
                fused_hi(1, k)
            split_hi(LATE // 2, 1, LATE + 1)
            spread_bias(LATE + 1)
            for t in range(2, TILES):
                mean(t)
                for k in range(HK):
                    fused_hi(t, k)
            with act.Fori(0, PAIRS) as j:
                for e in range(2):
                    split_hi(j + PAIRS, e, 2 * j + e, 2 * j + (TILES - 1) * RESIDENT + e + 1)
            with act.Fori(0, PAIRS) as j:
                for e in range(2):
                    split_hi(j + 2 * PAIRS, e, 2 * j + e, j * (2 * TILES) + PHASE1 + TILES * (e + 1))
            split_hi(CHUNKS // 2, 0, 0, PHASE1 + TILES * RESIDENT + TILES)

        @block.vector
        def _(dve):
            steps = [0]

            def then(instruction):
                steps[0] += 1
                instruction.then_inc(dve_step, 1)
                dve.wait_ge(dve_step, steps[0])

            def split_lo(e, slot, k, count):
                dve.wait_ge(hi_ready, count)
                nc.vector.tensor_tensor(w_lo[:, bass.ds(slot, 1), k, :], w_raw[:, e, k:k + 1, :],
                                        w_hi[:, bass.ds(slot, 1), k, :].bitcast(F32), ALU.subtract)\
                  .then_inc(lo_ready, 1)

            def sort(t):
                src = key[:, t, :]
                for n in range(PAD // 8):
                    top = key_sorted[:, 8 * n:8 * n + 8]
                    then(nc.vector.max(top, src))
                    if t == 0:
                        nc.vector.tensor_scalar(rows[:, t, 8 * n:8 * n + 8], top, -1.0, float(LAST),
                                                ALU.mult, ALU.add).then_inc(rows_ready, 1)
                    if n < PAD // 8 - 1:
                        rest = key_left[:, n % 2, :]
                        then(nc.vector.match_replace(out=rest, in_to_replace=top, in_values=src, imm_value=0.0))
                        src = rest
                if t:
                    nc.vector.tensor_scalar(rows[:, t, :], key_sorted[:], -1.0, float(LAST), ALU.mult, ALU.add)\
                      .then_inc(rows_ready, 1)
                dve.wait_ge(rows_ready, PAD // 8 + t)

            dve.wait_ge(idx_landed, 16)
            then(nc.vector.tensor_scalar(key, idx[:], 0.0, float(V), ALU.is_lt, ALU.mult))
            then(nc.vector.tensor_tensor(key, key, idx[:], ALU.add))
            then(nc.vector.tensor_scalar(key, key, 0.0, float(LAST), ALU.max, ALU.min))
            then(nc.vector.tensor_scalar(key, key, -1.0, float(LAST), ALU.mult, ALU.add))
            sort(0)
            then(nc.vector.tensor_scalar(flags, key, 0.0, None, ALU.is_gt))
            nc.vector.tensor_reduce(n_inner[:], flags, AX_X, ALU.add).then_inc(counted, 1)
            dve.wait_ge(counts_moved, 1)
            then(nc.vector.tensor_reduce(turns_f[:], small_ps[0:1, :].rearrange("a (t p) -> a t p", p=P), AX_X, ALU.max))
            then(nc.vector.tensor_scalar(turns_f[:], turns_f[:], float(TURN * MIN_TURNS), 1.0 / TURN,
                                         ALU.max, ALU.mult))
            then(nc.vector.tensor_scalar(turns_f[:], turns_f[:], 0.5 - 0.5 / TURN, ROUND_F32, ALU.add, ALU.add))
            then(nc.vector.tensor_scalar(turns_f[:], turns_f[:], ROUND_F32, None, ALU.subtract))
            nc.vector.tensor_copy(turns_i[:], turns_f[:]).then_inc(turns_ready, 1)
            dve.wait_ge(turns_spread, 1)
            then(nc.vector.tensor_scalar(n_left[:], small_ps[:, 0:TILES], -float(TURN), float(K),
                                         ALU.mult, ALU.add))

            def split_chunk(c):
                for k in range(HK):
                    split_lo(c % 2, c, k, HK * c + k + 1)

            for t in range(1, TILES):
                sort(t)
            split_chunk(0)

            def add_up(t, slots):
                if 0 in slots:
                    add_up.turns = dve.value_load(turns_i[0:1, t:t + 1], min_val=MIN_TURNS, max_val=K // TURN)
                    if t == 0:
                        dve.wait_ge(last_ready, 1)
                total = acc[:, t % 2, 0, :]
                for s in slots:
                    dve.wait_ge(gathered[t][s], add_up.turns * (16 * LAPS))
                    if s == 0:
                        then(nc.vector.scalar_tensor_tensor(total, last_row[:], n_left[:, t:t + 1], total,
                                                            ALU.mult, ALU.add))
                    elif s < ACC_SLOTS - 1:
                        then(nc.vector.tensor_tensor(total, total, acc[:, t % 2, s, :], ALU.add))
                    else:
                        nc.vector.tensor_tensor(total, total, acc[:, t % 2, s, :], ALU.add).then_inc(summed, 1)

            def fused_lo(t, k):
                dve.wait_ge(f_hi_ready, HK * t + k + 1)
                nc.vector.scalar_tensor_tensor(f_lo[:, t, k, :], fused_ps[k][:, t * P:(t + 1) * P],
                                               bf_col[:, k:k + 1], f_hi[:, t, k, :].bitcast(F32),
                                               ALU.add, ALU.subtract).then_inc(f_ready, 1)

            def evacuate(ps, group, slot, bias_slot, stored=None):
                dve.wait_ge(projected, group + 1)
                if stored is not None:
                    dve.wait_ge(out_stored[slot], stored)
                nc.vector.tensor_tensor(out_sb[:, slot:slot + 1, :], ps[:, 0:CHUNK].unsqueeze(1),
                                        bias[:, bass.ds(bias_slot, 1), 0:CHUNK], ALU.add).then_inc(evacuated, 1)

            def evacuate_first(c, group=None):
                group = c if group is None else group
                dve.wait_ge(bias_ready, c + 1)
                before = [out_slot(0, a) for a in range(c)].count(out_slot(0, c))
                evacuate(pair_ps[group % 2], group, out_slot(0, c), c, 16 * before if before else None)

            def evacuate_pair(t, j, parts=(0, 1)):
                for e in parts:
                    evacuate(pair_ps[e], t * RESIDENT + 2 * j + e, out_slot(t, e), 2 * j + e,
                             16 * (stored_before(t, e) + j))

            add_up(0, range(ACC_SLOTS))
            dve.wait_ge(bf_landed, 16)
            for k in range(HK):
                split_lo(1, 1, k, HK + k + 1)
                fused_lo(0, k)
            split_chunk(2)
            for c in range(TILES):
                evacuate_first(c)
                if c + EARLY < LATE:
                    split_chunk(c + EARLY)
            add_up(1, range(ACC_SLOTS))
            evacuate_first(TILES)
            split_chunk(LATE)
            evacuate_first(TILES + 1)
            for k in range(HK):
                fused_lo(1, k)
            split_chunk(LATE + 1)
            evacuate_first(RESIDENT - 2)
            evacuate(pair_ps[1], RESIDENT - 1, out_slot(1, 0), 0, 16 * stored_before(1, 0))
            evacuate_first(RESIDENT - 1, RESIDENT)
            evacuate_pair(1, 0, (1,))
            for t in range(1, TILES - 1):
                with dve.Fori(1 if t == 1 else 0, PAIRS - 2) as j:
                    evacuate_pair(t, j)
                add_up(t + 1, range(2))
                evacuate_pair(t, PAIRS - 2, (0,))
                add_up(t + 1, range(2, ACC_SLOTS))
                evacuate_pair(t, PAIRS - 2, (1,))
                evacuate_pair(t, PAIRS - 1, (0,))
                for k in range(HK):
                    fused_lo(t + 1, k)
                evacuate_pair(t, PAIRS - 1, (1,))
            for j in range(RESIDENT):
                evacuate_pair(TILES - 1, j // 2, (j % 2,))
                split_lo(j // HK, j // HK, j % HK, HK * RESIDENT + j + 1)

            def phase2(pair, e, ring, ring_ahead):
                c = 2 * pair + e
                dve.wait_ge(bias_landed, 16 * (c - RESIDENT + 1))
                for t in range(TILES):
                    evacuate(phase2_ps[t], TILES * c + t, t, 2 * ring + e,
                             16 * (c - RESIDENT + stored_before(TILES, t)))
                    if ring_ahead is not None:
                        split_lo(e, 2 * ring_ahead + e, t, HK * (c + AHEAD) + t + 1)

            phase2_all(dve, AHEAD, phase2)

        @block.tensor
        def _(pe):
            pe.wait_ge(ident_ready, 1)
            pe.wait_ge(user_landed, 16)
            for k in range(HK):
                for t in range(TILES):
                    m = nc.tensor.transpose(banks[k][:, t * P:(t + 1) * P], user_sb[:, t, k * P:(k + 1) * P], ident[:])
                m.then_inc(user_turned, 1)

            pe.wait_ge(counted, 1)
            for t in range(TILES):
                m = nc.tensor.matmul(small_ps[0:1, t * P:(t + 1) * P], n_inner[:, t:t + 1], ident[:],
                                     start=True, stop=True)
            m.then_inc(counts_moved, 1)
            pe.wait_ge(ones_ready, 1)
            pe.wait_ge(turns_ready, 1)
            nc.tensor.matmul(small_ps[:, 0:TILES], ones_row, turns_f[:], start=True, stop=True).then_inc(turns_spread, 1)

            pe.wait_ge(last_landed, 16)
            nc.tensor.matmul(pair_ps[0][:, :], ones_row, last_row[0:1, :], start=True, stop=True)\
              .then_inc(last_spread, 1)

            pe.wait_ge(user_t_ready, HK)
            pe.wait_ge(gathered[0][0], 16 * LAPS)
            pe.wait_ge(wf_user_landed, 16)
            for n in range(HK):
                for k in range(HK):
                    m = nc.tensor.matmul(fused_ps[n][:, :], wf_user[:, k, n * P:(n + 1) * P], user_t[:, k, :],
                                         start=(k == 0), stop=(k == HK - 1))
                m.then_inc(user_fused, 1)

            def spread_bias(c):
                if c == 0:
                    pe.wait_ge(bias_rows_landed, 16)
                if c > 2:
                    pe.wait_ge(bias_ready, c)
                nc.tensor.matmul(bias_ps(c)[:, 0:CHUNK], ident[0:RESIDENT, c:c + 1].to_broadcast([RESIDENT, P]),
                                 bias_rows, start=True, stop=True).then_inc(bias_spread, 1)

            def turn_sum(t):
                pe.wait_ge(summed, t + 1)
                if t:
                    pe.wait_ge(ret_ready, t)
                for k in range(HK):
                    m = nc.tensor.transpose(tr_ps[:, k * P:(k + 1) * P], acc[:, t % 2, 0, k * P:(k + 1) * P], ident[:])
                m.then_inc(ret_turned, 1)

            def fuse(t):
                pe.wait_ge(ret_ready, t + 1)
                if t == 0:
                    pe.wait_ge(wf_ret_landed, 16 * HK)
                for n in range(HK):
                    for k in range(HK):
                        m = nc.tensor.matmul(fused_ps[n][:, t * P:(t + 1) * P], wf_ret[:, k, n * P:(n + 1) * P],
                                             ret_t[:, k, :], start=False, stop=(k == HK - 1), skip_group_check=True)
                    m.then_inc(fused, 1)

            def project(t, slot, ps, free=None, halfway=None):
                if free is not None:
                    pe.wait_ge(evacuated, free)
                for k in range(HK):
                    if halfway and k == HK // 2:
                        halfway()
                    hi, lo = w_hi[:, bass.ds(slot, 1), k, :], w_lo[:, bass.ds(slot, 1), k, :]
                    for f, w, first in ((f_hi, hi, k == 0), (f_hi, lo, False), (f_lo, hi, False)):
                        m = nc.tensor.matmul(ps[:, 0:CHUNK].unsqueeze(1), f[:, t, k, :], w, start=first,
                                             stop=(f is f_lo and k == HK - 1))
                m.then_inc(projected, 1)

            def project_pair(t, j, parts=(0, 1), halfway=None):
                for e in parts:
                    project(t, 2 * j + e, pair_ps[e], t * RESIDENT + 2 * j + e - 1, halfway)

            turn_sum(0)
            fuse(0)
            for c in range(2):
                spread_bias(c)
            pe.wait_ge(f_ready, HK)
            for c in range(RESIDENT):
                if 2 <= c + 1 < RESIDENT:
                    spread_bias(c + 1)
                if c == LATE:
                    turn_sum(1)
                    fuse(1)
                if c < 2:
                    pe.wait_ge(bias_ready, c + 1)
                if c == RESIDENT - 1:
                    pe.wait_ge(f_ready, HK * 2)
                    project(1, 0, pair_ps[1], c - 1)
                pe.wait_ge(lo_ready, HK * (c + 1))
                group = c if c < RESIDENT - 1 else c + 1
                project(0, c, pair_ps[group % 2], group - 1 if c >= 2 else None)
            project_pair(1, 0, (1,))
            for t in range(1, TILES):
                pe.wait_ge(f_ready, HK * (t + 1))
                with pe.Fori(1 if t == 1 else 0, PAIRS - 1) as j:
                    project_pair(t, j)
                if t == TILES - 1:
                    project_pair(t, PAIRS - 1)
                else:
                    project_pair(t, PAIRS - 1, (0,), lambda: turn_sum(t + 1))
                    fuse(t + 1)
                    project_pair(t, PAIRS - 1, (1,))

            def phase2(c, slot):
                pe.wait_ge(lo_ready, HK * (c + 1))
                for t in range(TILES):
                    project(t, slot, phase2_ps[t], TILES * c + t - TILES + 1)

            for base in range(RESIDENT, CHUNKS - 1, RESIDENT):
                with pe.Fori(0, RESIDENT) as j:
                    phase2(base + j, j)
            phase2(CHUNKS - 1, 0)


_INS = ["r_user_rep", "r_indices", "L0_rec_item_embeddings", "L0_rec_W_fuse", "L0_rec_b_fuse", "L0_rec_W_proj",
        "L0_rec_b_proj"]


def kernel(**inputs):
    import numpy as np
    import concourse.bacc as bacc
    from concourse.bass_utils import run_bass_kernel_spmd

    nc = bacc.Bacc("TRN2", target_bir_lowering=False, num_devices=1, dynamic_dma_scratch_size=8192)
    arrays, args = {}, []
    for name in _INS:
        a = np.ascontiguousarray(inputs[name])
        arrays[name] = a
        args.append(nc.dram_tensor(name, a.shape, mybir.dt.from_np(a.dtype), kind="ExternalInput").ap())
    shape = (inputs["r_user_rep"].shape[0], inputs["L0_rec_W_proj"].shape[1])
    args.append(nc.dram_tensor("logits", shape, F32, kind="ExternalOutput").ap())
    retrieval_scores(nc, *args)
    r = run_bass_kernel_spmd(nc, [arrays], core_ids=[0])
    return r.results[0]["logits"]
```
